# Optimizing a Trainium2 kernel written in Bass

```python
import numpy as np
import jax
import jax.numpy as jnp

def _softmax(x, axis=-1):
    return jax.nn.softmax(x, axis=axis)

def _gelu(x):
    return jax.nn.gelu(x, approximate=True)

def _silu(x):
    return jax.nn.silu(x)

def _sigmoid(x):
    return jax.nn.sigmoid(x)

def _layernorm(x, axis=-1, eps=1e-05):
    m = jnp.mean(x, axis=axis, keepdims=True)
    v = jnp.var(x, axis=axis, keepdims=True)
    return (x - m) / jnp.sqrt(v + eps)

def _scatter_add(tgt, idx, src, axis=0):
    return tgt.at[idx].add(src)

def _segment_sum(src, seg, n):
    return jax.ops.segment_sum(src, seg, n)
kernel_name = 'mk_adaln_ffn_d1_seqx_r4_6cd185'

def setup_inputs(seed: int=0):
    np.random.seed(seed)
    _w = jnp.asarray

    def _rec_inputs():
        import jax
        import jax.numpy as jnp
        _rk = jax.random.key(seed)
        x = -7.109e-05 + 0.9999 * jax.random.normal(jax.random.fold_in(_rk, 1), (64, 64, 1024), jnp.float32)
        _lenS = 64 - jax.random.randint(jax.random.fold_in(_rk, 7), (64,), 0, max(1, 64 // 4) + 1, jnp.int32)
        _lenS2 = 64 - jax.random.randint(jax.random.fold_in(_rk, 8), (64,), 0, max(1, 64 // 4) + 1, jnp.int32)
        itok_B_0_15 = jax.random.randint(jax.random.fold_in(_rk, 11), (64,), 0, 16, jnp.int32)
        return (x, itok_B_0_15)
    x, itok_B_0_15 = _rec_inputs()

    def _L0_cond_setup():
        import jax, jax.numpy as jnp
        import numpy as np
        NUM_CONDITIONS = 16
        IN_CH = 64
        OUT_CH = 64
        B = 64
        T = 1024
        key = jax.random.key(seed)
        k_x, k_w, k_c = jax.random.split(key, 3)
        x = jax.random.normal(k_x, (B, IN_CH, T), dtype=jnp.float32)
        bound = float(np.sqrt(6.0 / IN_CH))
        weights = jax.random.uniform(k_w, (NUM_CONDITIONS, IN_CH, OUT_CH), dtype=jnp.float32, minval=-bound, maxval=bound)
        condition = jax.random.randint(k_c, (B,), 0, NUM_CONDITIONS, dtype=jnp.int64)
        return {'x': x, 'weights': weights, 'condition': condition}
    _L0_cond_all = _L0_cond_setup()
    _L0_cond_in = {k: v for k, v in _L0_cond_all.items() if k in ('weights',)}
    del _L0_cond_all

    def _L0_ffn_setup():
        import jax, jax.numpy as jnp
        import numpy as np
        IN_FEATURES = 1024

        def _dequantize(qweight, scale, zero_point):
            N, K_packed = qweight.shape
            groups = K_packed // 3
            p = qweight.reshape(N, groups, 3)
            v0 = p[:, :, 0] & 63
            v1 = p[:, :, 0] >> 6 & 63
            v2 = p[:, :, 1] & 63
            v3 = p[:, :, 2] & 63
            unpacked = jnp.stack([v0, v1, v2, v3], axis=2).reshape(N, groups * 4)
            unpacked = unpacked[:, :IN_FEATURES]
            return (unpacked.astype(jnp.float32) - zero_point) * scale
        key = jax.random.key(seed)
        k1, k2, k3, k4, k5 = jax.random.split(key, 5)
        x = jax.random.normal(k1, (8, 512, 1024), dtype=jnp.float32)
        qweight = jax.random.randint(k2, (1024, 768), 0, 1024, dtype=jnp.int32)
        weight_scale = jax.random.uniform(k3, (1024, 1), dtype=jnp.float32) * 0.02 + 0.001
        weight_zero_point = jax.random.uniform(k4, (1024, 1), dtype=jnp.float32) * 63.0
        bias = jax.random.normal(k5, (1024,), dtype=jnp.float32)
        return {'x': x, 'qweight': qweight, 'weight_scale': weight_scale, 'weight_zero_point': weight_zero_point, 'bias': bias}
    _L0_ffn_all = _L0_ffn_setup()
    _L0_ffn_in = {k: v for k, v in _L0_ffn_all.items() if k in ('qweight', 'weight_scale', 'weight_zero_point', 'bias')}
    del _L0_ffn_all
    return {'x': x, 'itok_B_0_15': itok_B_0_15, 'L0_cond_weights': _L0_cond_in['weights'], 'L0_ffn_qweight': _L0_ffn_in['qweight'], 'L0_ffn_weight_scale': _L0_ffn_in['weight_scale'], 'L0_ffn_weight_zero_point': _L0_ffn_in['weight_zero_point'], 'L0_ffn_bias': _L0_ffn_in['bias']}

def reference(x, itok_B_0_15, L0_cond_weights, L0_ffn_qweight, L0_ffn_weight_scale, L0_ffn_weight_zero_point, L0_ffn_bias):
    import jax
    import jax.numpy as jnp

    def _L0_cond_ref(x, weights, condition):
        import jax, jax.numpy as jnp
        import numpy as np
        NUM_CONDITIONS = 16
        IN_CH = 64
        OUT_CH = 64
        B = 64
        T = 1024
        W = weights[condition]
        return jnp.einsum('bct,bcd->bdt', x, W)

    def _L0_ffn_ref(x, qweight, weight_scale, weight_zero_point, bias):
        import jax, jax.numpy as jnp
        import numpy as np
        IN_FEATURES = 1024

        def _dequantize(qweight, scale, zero_point):
            N, K_packed = qweight.shape
            groups = K_packed // 3
            p = qweight.reshape(N, groups, 3)
            v0 = p[:, :, 0] & 63
            v1 = p[:, :, 0] >> 6 & 63
            v2 = p[:, :, 1] & 63
            v3 = p[:, :, 2] & 63
            unpacked = jnp.stack([v0, v1, v2, v3], axis=2).reshape(N, groups * 4)
            unpacked = unpacked[:, :IN_FEATURES]
            return (unpacked.astype(jnp.float32) - zero_point) * scale
        w = _dequantize(qweight, weight_scale, weight_zero_point)
        return jnp.einsum('bsk,nk->bsn', x, w) + bias
    x = x + _L0_ffn_ref(_L0_cond_ref(x, L0_cond_weights, itok_B_0_15), L0_ffn_qweight, L0_ffn_weight_scale, L0_ffn_weight_zero_point, L0_ffn_bias)
    return x

_drawn_inputs = setup_inputs


def setup_inputs(seed=0):
    import zlib

    import numpy as np

    out = dict(_drawn_inputs(seed))
    spreads = {}
    factors = {}
    for name, (base, spread) in spreads.items():
        noise = np.random.default_rng([zlib.crc32(name.encode()), seed]).standard_normal(out[name].shape)
        drawn = base * np.exp(spread * noise) if base else spread * noise
        out[name] = jnp.asarray(drawn.astype(out[name].dtype))
    for name, factor in factors.items():
        out[name] = (out[name] * factor).astype(out[name].dtype)
    return out
```

```python
from contextlib import ExitStack

import concourse.bass as bass
from concourse import mybir

ALU = mybir.AluOpType
ACT = mybir.ActivationFunctionType
F32 = mybir.dt.float32
F32R = mybir.dt.float32r
BF16 = mybir.dt.bfloat16
I32 = mybir.dt.int32

P = 128
QCENTER = 32.0
QMASK = 63
QBITS = 6


def adaln_ffn(nc: bass.Bass, x, cond, weights, qweight, scale, zero, bias, out):
    B, C, K = x.shape
    NCOND, _, S = weights.shape
    N, KP = qweight.shape
    assert C == S == P // 2 and N == K
    G = KP // 3
    KT = K // P
    NT = N // P
    H = 2
    NH = N // H
    TILES = B // 2
    RING = 4
    LEAD = 3
    LOADLEAD = LEAD + RING
    TRIPS = TILES // RING
    assert TILES % RING == 0

    x_rows = x.rearrange("b c k -> (b c) k")
    out_rows = out.rearrange("b s n -> (b s) n")

    with ExitStack() as ctx:
        def sb(name, shape, dt):
            return ctx.enter_context(nc.sbuf_tensor(name, shape, dt))

        def psum(name, shape, dt):
            return ctx.enter_context(nc.psum_tensor(name, shape, dt))

        def sem(name):
            return ctx.enter_context(nc.semaphore(name))

        ids = sb("ids", [1, B], I32)
        x_sb = sb("x_sb", [P, RING, K], F32)
        w_sb = sb("w_sb", [P, RING, P], F32)
        y_hi = sb("y_hi", [P, RING, KT, P], F32R)
        y_lo = sb("y_lo", [P, RING, KT, P], F32R)
        qT = sb("qT", [P, KT, N], F32R)
        q_raw = sb("q_raw", [P, NT, KP], I32)
        q_int = sb("q_int", [P, 2, G, 4], I32)
        q_bf = sb("q_bf", [P, 2, K], BF16)
        ident = sb("ident", [P, P], BF16)
        scale_bc = sb("scale_bc", [P, N], F32)
        bias_bc = sb("bias_bc", [P, N], F32)
        zs_bc = sb("zs_bc", [P, N], F32)
        xsum = sb("xsum", [P, RING], F32)
        ysum = sb("ysum", [P, RING], F32)
        junk = sb("junk", [P, K], BF16)
        resid = sb("resid", [P, RING, N], F32)
        o_sb = sb("o_sb", [P, 2, N], F32)

        y_ps = psum("y_ps", [P, 2, KT, P], F32)
        o_ps = psum("o_ps", [P, H, NH], F32)
        ysum_ps = psum("ysum_ps", [P, 512], F32)
        qt_ps = psum("qt_ps", [P, KT, P], BF16)

        ids_loaded = sem("ids_loaded")
        x_loaded = [sem(f"x_loaded{s}") for s in range(RING)]
        w_loaded = [sem(f"w_loaded{s}") for s in range(RING)]
        q_loaded = [sem(f"q_loaded{n}") for n in range(NT)]
        scale_loaded = sem("scale_loaded")
        zero_loaded = sem("zero_loaded")
        bias_loaded = sem("bias_loaded")
        w_zeroed = sem("w_zeroed")
        blank_ready = sem("blank_ready")
        ident_ready = sem("ident_ready")
        zs_part = sem("zs_part")
        q_part = sem("q_part")
        q_cast = sem("q_cast")
        qt_ps_ready = sem("qt_ps_ready")
        qt_ready = sem("qt_ready")
        y_ps_ready = sem("y_ps_ready")
        y_hi_ready = sem("y_hi_ready")
        y_lo_ready = sem("y_lo_ready")
        xsum_ready = sem("xsum_ready")
        ysum_ps_ready = sem("ysum_ps_ready")
        ysum_ready = sem("ysum_ready")
        xbias_ready = sem("xbias_ready")
        resid_ready = sem("resid_ready")
        o_ps_ready = sem("o_ps_ready")
        scaled = sem("scaled")
        o_ready = sem("o_ready")
        o_stored = [sem(f"o_stored{s}") for s in range(2)]

        block = ctx.enter_context(nc.Block())

        def x_arrived(eng, j, i):
            eng.wait_ge(x_loaded[j % RING], (i + j // RING + 1) * 16)

        @block.sync
        def _(sp):
            def load_x(j, i):
                t = i * RING + j
                sp.dma_start(x_sb[:, j % RING, :],
                             x_rows[bass.ds(t * P, P), :]).then_inc(x_loaded[j % RING], 16)

            def load_w(j, i):
                t = i * RING + j
                for half in range(2):
                    c = sp.value_load(ids[0:1, bass.ds(t * 2 + half, 1)], min_val=0, max_val=NCOND - 1)
                    rows = slice(half * S, (half + 1) * S)
                    sp.dma_start(w_sb[rows, j % RING, rows],
                                 weights[bass.ds(c, 1), :, :].rearrange("a c s -> (a c) s")
                                 ).then_inc(w_loaded[j % RING], 16)

            def reload(j, i):
                old = i * RING + j - RING + 1
                sp.wait_ge(y_ps_ready, old * 2)
                sp.wait_ge(ysum_ps_ready, old)
                sp.wait_ge(xsum_ready, old)
                sp.wait_ge(xbias_ready, old)
                load_x(j, i)
                load_w(j, i)

            def store(j, i):
                t = i * RING + j
                for h in range(H):
                    sp.wait_ge(o_ready, t * H + h + 1)
                    sp.dma_start(out_rows[bass.ds(t * P, P), h * NH:(h + 1) * NH],
                                 o_sb[:, j % 2, h * NH:(h + 1) * NH]).then_inc(o_stored[j % 2], 16)

            def load_q(n):
                sp.dma_start(q_raw[:, n, :], qweight[n * P:(n + 1) * P, :]).then_inc(q_loaded[n], 16)

            def load_row(dst, src, s):
                sp.dma_start(dst[:], src.partition_broadcast(P)).then_inc(s, 16)

            sp.dma_start(ids[:], cond.rearrange("(a b) -> a b", a=1)).then_inc(ids_loaded, 16)
            load_q(0)
            load_x(0, 0)
            load_q(1)
            sp.wait_ge(ids_loaded, 16)
            sp.wait_ge(w_zeroed, 1)
            load_w(0, 0)
            load_q(2)
            load_q(3)
            load_x(1, 0)
            load_w(1, 0)
            for n in range(4, NT):
                load_q(n)
            load_x(2, 0)
            load_w(2, 0)
            load_x(3, 0)
            load_w(3, 0)
            load_row(zs_bc, zero.rearrange("n a -> (n a)"), zero_loaded)
            load_row(scale_bc, scale.rearrange("n a -> (n a)"), scale_loaded)
            load_row(bias_bc, bias, bias_loaded)
            for j in range(RING, LOADLEAD):
                reload(j, 0)

            def step(j, i, loads=True):
                if loads:
                    reload(j + LOADLEAD, i)
                store(j, i)

            with sp.Fori(0, TRIPS - 2) as i:
                for j in range(RING):
                    step(j, i)
            for t in range(TILES - 2 * RING, TILES):
                step(t % RING, t // RING, loads=t + LOADLEAD < TILES)
            for s in range(2):
                sp.wait_ge(o_stored[s], 16 * H * TILES // 2)

        @block.tensor
        def _(pe):
            def mix(j, i):
                t = i * RING + j
                slot = j % RING
                x_arrived(pe, j, i)
                pe.wait_ge(w_loaded[slot], (i + j // RING + 1) * 32)
                if not isinstance(t, int) or t >= 2:
                    pe.wait_ge(y_lo_ready, (t - 1) * 2)
                pe.wait_ge(xsum_ready, t + 1)
                if not isinstance(t, int) or t >= 1:
                    pe.wait_ge(ysum_ready, t)
                for kt in range(KT):
                    last = nc.tensor.matmul(y_ps[:, j % 2, kt, :], x_sb[:, slot, kt * P:(kt + 1) * P],
                                            w_sb[:, slot, :], start=True, stop=True)
                    if kt % (KT // 2) == KT // 2 - 1:
                        last.then_inc(y_ps_ready, 1)
                nc.tensor.matmul(ysum_ps[:, slot:slot + 1], w_sb[:, slot, :], xsum[:, slot:slot + 1],
                                 start=True, stop=True).then_inc(ysum_ps_ready, 1)

            def transpose_q(n):
                pe.wait_ge(q_cast, n + 1)
                if n >= 1:
                    pe.wait_ge(qt_ready, n)
                for kt in range(KT):
                    last = nc.tensor.transpose(qt_ps[:, kt, :], q_bf[:, n % 2, kt * P:(kt + 1) * P], ident[:])
                last.then_inc(qt_ps_ready, 1)

            def linear(j, i, h):
                t = i * RING + j
                if h == 0:
                    pe.wait_ge(y_lo_ready, t * 2 + 2)
                if not isinstance(t, int) or t >= 1:
                    pe.wait_ge(scaled, t * H - H + h + 1)
                for kt in range(KT):
                    for part in (y_hi, y_lo):
                        last = nc.tensor.matmul(o_ps[:, h, :], part[:, j % RING, kt, :],
                                                qT[:, kt, h * NH:(h + 1) * NH],
                                                start=(kt == 0 and part is y_hi),
                                                stop=(kt == KT - 1 and part is y_lo))
                last.then_inc(o_ps_ready, 1)

            def step(j, i, mixes=True):
                if mixes:
                    mix(j + LEAD, i)
                for h in range(H):
                    linear(j, i, h)

            pe.wait_ge(ident_ready, 1)
            mix(0, 0)
            transpose_q(0)
            transpose_q(1)
            mix(1, 0)
            transpose_q(2)
            transpose_q(3)
            mix(2, 0)
            mix(3, 0)
            pe.wait_ge(qt_ready, NT // 2)
            linear(0, 0, 0)
            for n in range(NT // 2, NT):
                transpose_q(n)
            pe.wait_ge(qt_ready, NT)
            linear(0, 0, 1)
            for j in range(1, RING):
                step(j, 0)
            with pe.Fori(1, TRIPS - 1) as i:
                for j in range(RING):
                    step(j, i)
            for j in range(RING):
                step(j, TRIPS - 1, mixes=j + LEAD < RING)

        @block.scalar
        def _(act):
            def sum_x(j, i):
                x_arrived(act, j, i)
                if not isinstance(i, int) or i * RING + j >= RING:
                    act.wait_ge(ysum_ps_ready, i * RING + j - RING + 1)
                nc.scalar.activation(junk[:], x_sb[:, j % RING, :], ACT.Copy,
                                     accum_out=xsum[:, j % RING:j % RING + 1]).then_inc(xsum_ready, 1)

            def high(j, i):
                t = i * RING + j
                for half in range(2):
                    act.wait_ge(y_ps_ready, t * 2 + half + 1)
                    chunks = slice(half * KT // 2, (half + 1) * KT // 2)
                    nc.scalar.activation(y_hi[:, j % RING, chunks, :], y_ps[:, j % 2, chunks, :],
                                         ACT.Copy).then_inc(y_hi_ready, 1)
                act.wait_ge(ysum_ps_ready, t + 1)
                if not isinstance(t, int) or t >= RING:
                    act.wait_ge(resid_ready, t - RING + 1)
                nc.scalar.activation(ysum[:, j % RING:j % RING + 1], ysum_ps[:, j % RING:j % RING + 1],
                                     ACT.Copy).then_inc(ysum_ready, 1)

            def cast_q(n):
                act.wait_ge(q_part, 3 * (n + 1))
                if n >= 2:
                    act.wait_ge(qt_ps_ready, n - 1)
                nc.scalar.activation(q_bf[:, n % 2, :], q_int[:, n % 2, :, :].rearrange("p g j -> p (g j)"),
                                     ACT.Copy, bias=-QCENTER).then_inc(q_cast, 1)

            sum_x(0, 0)
            cast_q(0)
            high(0, 0)
            cast_q(1)
            sum_x(1, 0)
            cast_q(2)
            high(1, 0)
            cast_q(3)
            sum_x(2, 0)
            high(2, 0)
            cast_q(4)
            sum_x(3, 0)
            high(3, 0)
            for n in range(5, NT):
                cast_q(n)
            sum_x(4, 0)

            def step(j, i, highs=True, sums=True):
                if highs:
                    high(j + LEAD, i)
                if sums:
                    sum_x(j + LEAD + 1, i)

            for j in range(1, RING):
                step(j, 0)
            with act.Fori(1, TRIPS - 1) as i:
                for j in range(RING):
                    step(j, i)
            step(0, TRIPS - 1, sums=False)

        @block.vector
        def _(dve):
            def unpack_q(n):
                dve.wait_ge(q_loaded[n], 16)
                if n >= 2:
                    dve.wait_ge(q_cast, n - 1)
                words = q_raw[:, n, :].rearrange("p (g w) -> p g w", w=3)
                to = q_int[:, n % 2, :, :]
                nc.vector.tensor_scalar(to[:, :, 0], words[:, :, 0], QMASK, None,
                                        ALU.bitwise_and).then_inc(q_part, 1)
                nc.vector.tensor_scalar(to[:, :, 1], words[:, :, 0], QBITS, QMASK,
                                        ALU.logical_shift_right, ALU.bitwise_and).then_inc(q_part, 1)
                nc.vector.tensor_scalar(to[:, :, 2:4], words[:, :, 1:3], QMASK, None,
                                        ALU.bitwise_and).then_inc(q_part, 1)

            def place_q(n):
                dve.wait_ge(qt_ps_ready, n + 1)
                nc.vector.tensor_copy(qT[:, :, n * P:(n + 1) * P], qt_ps[:, :, :]).then_inc(qt_ready, 1)

            def low(j, i):
                t = i * RING + j
                for half in range(2):
                    dve.wait_ge(y_hi_ready, t * 2 + half + 1)
                    chunks = slice(half * KT // 2, (half + 1) * KT // 2)
                    nc.vector.tensor_tensor(y_lo[:, j % RING, chunks, :], y_ps[:, j % 2, chunks, :],
                                            y_hi[:, j % RING, chunks, :].bitcast(F32),
                                            ALU.subtract).then_inc(y_lo_ready, 1)

            def residual(j, i):
                t = i * RING + j
                dve.wait_ge(xbias_ready, t + 1)
                dve.wait_ge(ysum_ready, t + 1)
                nc.vector.scalar_tensor_tensor(resid[:, j % RING, :], zs_bc[:], ysum[:, j % RING:j % RING + 1],
                                               resid[:, j % RING, :], ALU.mult, ALU.add).then_inc(resid_ready, 1)

            def finish(j, i):
                t = i * RING + j
                for h in range(H):
                    cols = slice(h * NH, (h + 1) * NH)
                    dve.wait_ge(o_ps_ready, t * H + h + 1)
                    if h == 0 and (not isinstance(i, int) or i * RING + j >= 2):
                        dve.wait_ge(o_stored[j % 2], (t // 2 if isinstance(t, int) else i * (RING // 2) + j // 2) * 16 * H)
                    nc.vector.tensor_tensor(o_sb[:, j % 2, cols], o_ps[:, h, :], scale_bc[:, cols],
                                            ALU.mult).then_inc(scaled, 1)
                    dve.wait_ge(scaled, t * H + h + 1)
                    if h == 0:
                        dve.wait_ge(resid_ready, t + 1)
                    nc.vector.tensor_tensor(o_sb[:, j % 2, cols], o_sb[:, j % 2, cols],
                                            resid[:, j % RING, cols], ALU.add).then_inc(o_ready, 1)

            unpack_q(0)
            unpack_q(1)
            low(0, 0)
            place_q(0)
            unpack_q(2)
            place_q(1)
            unpack_q(3)
            low(1, 0)
            place_q(2)
            unpack_q(4)
            place_q(3)
            low(2, 0)
            unpack_q(5)
            low(3, 0)
            for n in range(4, NT):
                if n + 2 < NT:
                    unpack_q(n + 2)
                place_q(n)
            dve.wait_ge(zero_loaded, 16)
            nc.vector.tensor_scalar(zs_bc[:], zs_bc[:], -1.0, QCENTER, ALU.mult, ALU.add).then_inc(zs_part, 1)
            dve.wait_ge(zs_part, 1)
            dve.wait_ge(scale_loaded, 16)
            nc.vector.tensor_tensor(zs_bc[:], zs_bc[:], scale_bc[:], ALU.mult).then_inc(zs_part, 1)
            dve.wait_ge(zs_part, 2)

            def step(j, i, lows=True):
                if lows:
                    low(j + LEAD, i)
                residual(j, i)
                finish(j, i)

            step(0, 0, lows=False)
            for j in range(1, RING):
                step(j, 0)
            with dve.Fori(1, TRIPS - 1) as i:
                for j in range(RING):
                    step(j, i)
            for j in range(RING):
                step(j, TRIPS - 1, lows=j + LEAD < RING)

        @block.gpsimd
        def _(pool):
            nc.gpsimd.memset(w_sb[:], 0.0).then_inc(w_zeroed, 1)
            nc.gpsimd.memset(ident[:], 0.0).then_inc(blank_ready, 1)
            pool.wait_ge(blank_ready, 1)
            nc.gpsimd.affine_select(out=ident[:], in_=ident[:], compare_op=ALU.not_equal, fill=1.0, base=0,
                                    pattern=[[-1, P]], channel_multiplier=1).then_inc(ident_ready, 1)
            pool.wait_ge(bias_loaded, 16)

            def add_bias(j, i):
                x_arrived(pool, j, i)
                if not isinstance(i, int) or i * RING + j >= RING:
                    pool.wait_ge(o_ready, (i * RING + j - RING + 1) * H)
                nc.gpsimd.tensor_tensor(resid[:, j % RING, :], x_sb[:, j % RING, :], bias_bc[:],
                                        ALU.add).then_inc(xbias_ready, 1)

            for j in range(RING):
                add_bias(j, 0)
            with pool.Fori(1, TRIPS) as i:
                for j in range(RING):
                    add_bias(j, i)


_INS = ['x', 'itok_B_0_15', 'L0_cond_weights', 'L0_ffn_qweight', 'L0_ffn_weight_scale',
        'L0_ffn_weight_zero_point', 'L0_ffn_bias']


def kernel(**inputs):
    import numpy as _np
    import concourse.bacc as _bacc
    from concourse import mybir as _mybir
    from concourse.bass_utils import run_bass_kernel_spmd as _run

    nc = _bacc.Bacc("TRN2", target_bir_lowering=False, num_devices=1)
    arrays, args = {}, []
    for name in _INS:
        a = _np.ascontiguousarray(inputs[name])
        arrays[f"in_{name}_dram"] = a
        args.append(nc.dram_tensor(f"in_{name}_dram", a.shape, _mybir.dt.from_np(a.dtype), kind="ExternalInput").ap())
    args.append(nc.dram_tensor("out_0_dram", inputs["x"].shape, _mybir.dt.float32, kind="ExternalOutput").ap())
    adaln_ffn(nc, *args)
    r = _run(nc, [arrays], core_ids=[0])
    return r.results[0]["out_0_dram"]
```

```python
from contextlib import ExitStack

import concourse.bass as bass
from concourse import mybir

ALU = mybir.AluOpType
ACT = mybir.ActivationFunctionType
F32 = mybir.dt.float32
F32R = mybir.dt.float32r
BF16 = mybir.dt.bfloat16
I32 = mybir.dt.int32
I16 = mybir.dt.int16

P = 128
WARMUP = 20
QCENTER = 32.0
QMASK = 63
QBITS = 6


def adaln_ffn(nc: bass.Bass, x, cond, weights, qweight, scale, zero, bias, out):
    B, C, K = x.shape
    NCOND, _, S = weights.shape
    N, KP = qweight.shape
    assert C == S == P // 2 and N == K
    G = KP // 3
    KT = K // P
    NT = N // P
    H = 2
    NH = N // H
    TILES = B // 2
    RING = 4
    LEAD = 3
    LOADLEAD = LEAD + RING
    TRIPS = TILES // RING
    assert TILES % RING == 0

    x_rows = x.rearrange("b c k -> (b c) k")
    out_rows = out.rearrange("b s n -> (b s) n")

    with ExitStack() as ctx:
        def sb(name, shape, dt):
            return ctx.enter_context(nc.sbuf_tensor(name, shape, dt))

        def psum(name, shape, dt):
            return ctx.enter_context(nc.psum_tensor(name, shape, dt))

        def sem(name):
            return ctx.enter_context(nc.semaphore(name))

        ids = sb("ids", [1, B], I32)
        x_sb = sb("x_sb", [P, RING, K], F32)
        w_sb = sb("w_sb", [P, RING, P], F32)
        y_hi = sb("y_hi", [P, RING, KT, P], F32R)
        y_lo = sb("y_lo", [P, RING, KT, P], F32R)
        qT = sb("qT", [P, KT, N], F32R)
        q_raw = sb("q_raw", [P, NT, KP], I32)
        q_int = sb("q_int", [P, 2, G, 4], I16)
        q_bf = sb("q_bf", [P, 4, K], BF16)
        ident = sb("ident", [P, P], BF16)
        scale_bc = sb("scale_bc", [P, N], F32)
        bias_bc = sb("bias_bc", [P, N], F32)
        zs_bc = sb("zs_bc", [P, N], F32)
        xsum = sb("xsum", [P, RING], F32)
        ysum = sb("ysum", [P, RING], F32)
        warm = sb("warm", [P, 512], BF16)
        junk = sb("junk", [P, K], BF16)
        resid = sb("resid", [P, RING, N], F32)
        o_sb = sb("o_sb", [P, 2, N], F32)

        y_ps = psum("y_ps", [P, 2, KT, P], F32)
        o_ps = psum("o_ps", [P, H, NH], F32)
        ysum_ps = psum("ysum_ps", [P, 512], F32)
        qt_ps = psum("qt_ps", [P, KT, P], BF16)
        qt_banks = [qt_ps[:, :, :], o_ps[:, 1, :].bitcast(BF16).rearrange("p (t n) -> p t n", t=KT)]

        ids_loaded = sem("ids_loaded")
        x_loaded = [sem(f"x_loaded{s}") for s in range(RING)]
        w_loaded = [sem(f"w_loaded{s}") for s in range(RING)]
        q_loaded = [sem(f"q_loaded{n}") for n in range(NT)]
        scale_loaded = sem("scale_loaded")
        zero_loaded = sem("zero_loaded")
        bias_loaded = sem("bias_loaded")
        w_zeroed = sem("w_zeroed")
        blank_ready = sem("blank_ready")
        ident_ready = sem("ident_ready")
        zs_part = sem("zs_part")
        q_part = sem("q_part")
        q_cast = sem("q_cast")
        qt_ps_ready = sem("qt_ps_ready")
        qt_ready = [sem(f"qt_ready{e}") for e in range(2)]
        warm_ready = sem("warm_ready")
        y_ps_ready = sem("y_ps_ready")
        y_hi_ready = sem("y_hi_ready")
        y_lo_ready = sem("y_lo_ready")
        xsum_ready = sem("xsum_ready")
        ysum_ps_ready = sem("ysum_ps_ready")
        ysum_ready = sem("ysum_ready")
        xbias_ready = sem("xbias_ready")
        resid_ready = sem("resid_ready")
        o_ps_ready = [sem(f"o_ps_ready{h}") for h in range(H)]
        scaled = [sem(f"scaled{h}") for h in range(H)]
        o_ready = [sem(f"o_ready{h}") for h in range(H)]
        o_stored = [[sem(f"o_stored{h}_{s}") for s in range(2)] for h in range(H)]

        block = ctx.enter_context(nc.Block())

        def x_arrived(eng, j, i):
            eng.wait_ge(x_loaded[j % RING], (i + j // RING + 1) * 16)

        @block.sync
        def _(sp):
            def load_x(j, i):
                t = i * RING + j
                sp.dma_start(x_sb[:, j % RING, :],
                             x_rows[bass.ds(t * P, P), :]).then_inc(x_loaded[j % RING], 16)

            def load_w(j, i):
                t = i * RING + j
                picked = [sp.value_load(ids[0:1, bass.ds(t * 2 + half, 1)], min_val=0, max_val=NCOND - 1)
                          for half in range(2)]
                for half in range(2):
                    rows = slice(half * S, (half + 1) * S)
                    sp.dma_start(w_sb[rows, j % RING, rows],
                                 weights[bass.ds(picked[half], 1), :, :].rearrange("a c s -> (a c) s")
                                 ).then_inc(w_loaded[j % RING], 16)

            def reload(j, i):
                old = i * RING + j - RING + 1
                sp.wait_ge(y_ps_ready, old * 2)
                sp.wait_ge(ysum_ps_ready, old)
                sp.wait_ge(xsum_ready, old)
                sp.wait_ge(xbias_ready, old)
                load_x(j, i)
                load_w(j, i)

            def store(j, i, h):
                t = i * RING + j
                sp.wait_ge(o_ready[h], t + 1)
                sp.dma_start(out_rows[bass.ds(t * P, P), h * NH:(h + 1) * NH],
                             o_sb[:, j % 2, h * NH:(h + 1) * NH]).then_inc(o_stored[h][j % 2], 16)

            def load_q(n):
                sp.dma_start(q_raw[:, n, :], qweight[n * P:(n + 1) * P, :]).then_inc(q_loaded[n], 16)

            def load_row(dst, src, s):
                sp.dma_start(dst[:], src.partition_broadcast(P)).then_inc(s, 16)

            sp.dma_start(ids[:], cond.rearrange("(a b) -> a b", a=1)).then_inc(ids_loaded, 16)
            load_x(0, 0)
            load_q(0)
            load_q(1)
            sp.wait_ge(ids_loaded, 16)
            sp.wait_ge(w_zeroed, 1)
            load_w(0, 0)
            load_x(1, 0)
            load_q(2)
            load_w(1, 0)
            load_q(3)
            load_row(scale_bc, scale.rearrange("n a -> (n a)"), scale_loaded)
            load_x(2, 0)
            load_q(4)
            load_w(2, 0)
            for n in range(5, NT):
                load_q(n)
            load_row(zs_bc, zero.rearrange("n a -> (n a)"), zero_loaded)
            load_row(bias_bc, bias, bias_loaded)
            load_x(3, 0)
            load_w(3, 0)

            for j in range(3):
                reload(j + RING, 0)
                store(j, 0, 0)
            for j in range(3):
                store(j, 0, 1)
                reload(j + LOADLEAD, 0)

            def step(j, i, loads=True):
                if loads:
                    reload(j + LOADLEAD, i)
                for h in range(H):
                    store(j, i, h)

            step(3, 0)
            with sp.Fori(1, TRIPS - 2) as i:
                for j in range(RING):
                    step(j, i)
            for t in range(TILES - 2 * RING, TILES):
                step(t % RING, t // RING, loads=t + LOADLEAD < TILES)
            for h in range(H):
                for s in range(2):
                    sp.wait_ge(o_stored[h][s], 16 * TILES // 2)

        @block.tensor
        def _(pe):
            def mix(j, i):
                t = i * RING + j
                slot = j % RING
                x_arrived(pe, j, i)
                pe.wait_ge(w_loaded[slot], (i + j // RING + 1) * 32)
                if not isinstance(t, int) or t >= 2:
                    pe.wait_ge(y_lo_ready, (t - 1) * 2)
                pe.wait_ge(xsum_ready, t + 1)
                if not isinstance(t, int) or t >= 1:
                    pe.wait_ge(ysum_ready, t)
                for kt in range(KT):
                    last = nc.tensor.matmul(y_ps[:, j % 2, kt, :], x_sb[:, slot, kt * P:(kt + 1) * P],
                                            w_sb[:, slot, :], start=True, stop=True)
                    if kt % (KT // 2) == KT // 2 - 1:
                        last.then_inc(y_ps_ready, 1)
                nc.tensor.matmul(ysum_ps[:, slot:slot + 1], w_sb[:, slot, :], xsum[:, slot:slot + 1],
                                 start=True, stop=True).then_inc(ysum_ps_ready, 1)

            def transpose_q(n):
                pe.wait_ge(q_cast, n + 1)
                if n >= 2:
                    pe.wait_ge(qt_ready[n % 2], n // 2)
                for kt in range(KT):
                    last = nc.tensor.transpose(qt_banks[n % 2][:, kt, :], q_bf[:, n % 4, kt * P:(kt + 1) * P],
                                               ident[:])
                last.then_inc(qt_ps_ready, 1)

            def linear(j, i, h):
                t = i * RING + j
                if h == 0:
                    pe.wait_ge(y_lo_ready, t * 2 + 2)
                if not isinstance(t, int) or t >= 1:
                    pe.wait_ge(scaled[h], t)
                for kt in range(KT):
                    for part in (y_hi, y_lo):
                        last = nc.tensor.matmul(o_ps[:, h, :], part[:, j % RING, kt, :],
                                                qT[:, kt, h * NH:(h + 1) * NH],
                                                start=(kt == 0 and part is y_hi),
                                                stop=(kt == KT - 1 and part is y_lo))
                last.then_inc(o_ps_ready[h], 1)

            def step(j, i, mixes=True):
                if mixes:
                    mix(j + LEAD, i)
                for h in range(H):
                    linear(j, i, h)

            pe.wait_ge(warm_ready, 1)
            for _ in range(WARMUP):
                nc.tensor.matmul(ysum_ps[:], warm[:, 0:P], warm[:], start=True, stop=True)
            mix(0, 0)
            pe.wait_ge(ident_ready, 1)
            transpose_q(0)
            transpose_q(1)
            mix(1, 0)
            transpose_q(2)
            transpose_q(3)
            for e in range(2):
                pe.wait_ge(qt_ready[e], NT // 4)
            linear(0, 0, 0)
            mix(2, 0)
            transpose_q(4)
            transpose_q(5)
            linear(1, 0, 0)
            transpose_q(6)
            transpose_q(7)
            linear(2, 0, 0)
            mix(3, 0)
            for e in range(2):
                pe.wait_ge(qt_ready[e], NT // 2)
            for j in range(3):
                linear(j, 0, 1)
                mix(j + RING, 0)
            for h in range(H):
                linear(3, 0, h)
            with pe.Fori(1, TRIPS - 1) as i:
                for j in range(RING):
                    step(j, i)
            for j in range(RING):
                step(j, TRIPS - 1, mixes=j + LEAD < RING)

        @block.scalar
        def _(act):
            def sum_x(j, i):
                x_arrived(act, j, i)
                if not isinstance(i, int) or i * RING + j >= RING:
                    act.wait_ge(ysum_ps_ready, i * RING + j - RING + 1)
                nc.scalar.activation(junk[:], x_sb[:, j % RING, :], ACT.Copy,
                                     accum_out=xsum[:, j % RING:j % RING + 1]).then_inc(xsum_ready, 1)

            def high(j, i):
                t = i * RING + j
                for half in range(2):
                    act.wait_ge(y_ps_ready, t * 2 + half + 1)
                    chunks = slice(half * KT // 2, (half + 1) * KT // 2)
                    nc.scalar.activation(y_hi[:, j % RING, chunks, :], y_ps[:, j % 2, chunks, :],
                                         ACT.Copy).then_inc(y_hi_ready, 1)
                act.wait_ge(ysum_ps_ready, t + 1)
                if not isinstance(t, int) or t >= RING:
                    act.wait_ge(resid_ready, t - RING + 1)
                nc.scalar.activation(ysum[:, j % RING:j % RING + 1], ysum_ps[:, j % RING:j % RING + 1],
                                     ACT.Copy).then_inc(ysum_ready, 1)

            def place_q(n):
                act.wait_ge(qt_ps_ready, n + 1)
                nc.scalar.activation(qT[:, :, n * P:(n + 1) * P], qt_banks[0], ACT.Copy).then_inc(qt_ready[0], 1)

            sum_x(0, 0)
            high(0, 0)
            place_q(0)
            sum_x(1, 0)
            place_q(2)
            high(1, 0)
            sum_x(2, 0)
            high(2, 0)
            place_q(4)
            place_q(6)
            sum_x(3, 0)
            high(3, 0)
            sum_x(4, 0)

            def step(j, i, highs=True, sums=True):
                if highs:
                    high(j + LEAD, i)
                if sums:
                    sum_x(j + LEAD + 1, i)

            for j in range(1, RING):
                step(j, 0)
            with act.Fori(1, TRIPS - 1) as i:
                for j in range(RING):
                    step(j, i)
            step(0, TRIPS - 1, sums=False)

        @block.vector
        def _(dve):
            def unpack_q(n):
                dve.wait_ge(q_loaded[n], 16)
                words = q_raw[:, n, :].bitcast(I16).rearrange("p (g w e) -> p g w e", w=3, e=2)
                to = q_int[:, n % 2, :, :]
                if n >= 2:
                    dve.wait_ge(q_cast, n - 1)
                nc.vector.tensor_scalar(to[:, :, 0], words[:, :, 0, 0], QMASK, None,
                                        ALU.bitwise_and).then_inc(q_part, 1)
                nc.vector.tensor_scalar(to[:, :, 1], words[:, :, 0, 0], QBITS, QMASK,
                                        ALU.logical_shift_right, ALU.bitwise_and).then_inc(q_part, 1)
                nc.vector.tensor_scalar(to[:, :, 2:4], words[:, :, 1:3, 0], QMASK, None,
                                        ALU.bitwise_and).then_inc(q_part, 1)
                dve.wait_ge(q_part, 3 * (n + 1))
                if n >= 4:
                    dve.wait_ge(qt_ps_ready, n - 3)
                nc.vector.tensor_scalar(q_bf[:, n % 4, :], to.rearrange("p g j -> p (g j)"), QCENTER, None,
                                        ALU.subtract).then_inc(q_cast, 1)

            def low(j, i):
                t = i * RING + j
                for half in range(2):
                    dve.wait_ge(y_hi_ready, t * 2 + half + 1)
                    chunks = slice(half * KT // 2, (half + 1) * KT // 2)
                    nc.vector.tensor_tensor(y_lo[:, j % RING, chunks, :], y_ps[:, j % 2, chunks, :],
                                            y_hi[:, j % RING, chunks, :].bitcast(F32),
                                            ALU.subtract).then_inc(y_lo_ready, 1)

            def residual(j, i):
                t = i * RING + j
                dve.wait_ge(xbias_ready, t + 1)
                dve.wait_ge(ysum_ready, t + 1)
                nc.vector.scalar_tensor_tensor(resid[:, j % RING, :], zs_bc[:], ysum[:, j % RING:j % RING + 1],
                                               resid[:, j % RING, :], ALU.mult, ALU.add).then_inc(resid_ready, 1)

            def scale_out(j, i, h):
                t = i * RING + j
                cols = slice(h * NH, (h + 1) * NH)
                dve.wait_ge(o_ps_ready[h], t + 1)
                if not isinstance(i, int):
                    dve.wait_ge(o_stored[h][j % 2], (i * (RING // 2) + j // 2) * 16)
                elif t >= 2:
                    dve.wait_ge(o_stored[h][j % 2], t // 2 * 16)
                nc.vector.tensor_tensor(o_sb[:, j % 2, cols], o_ps[:, h, :], scale_bc[:, cols],
                                        ALU.mult).then_inc(scaled[h], 1)

            def add_residual(j, i, h):
                t = i * RING + j
                cols = slice(h * NH, (h + 1) * NH)
                dve.wait_ge(scaled[h], t + 1)
                dve.wait_ge(resid_ready, t + 1)
                nc.vector.tensor_tensor(o_sb[:, j % 2, cols], o_sb[:, j % 2, cols],
                                        resid[:, j % RING, cols], ALU.add).then_inc(o_ready[h], 1)

            def finish(j, i, h):
                scale_out(j, i, h)
                add_residual(j, i, h)

            def place_q(n):
                dve.wait_ge(qt_ps_ready, n + 1)
                nc.vector.tensor_copy(qT[:, :, n * P:(n + 1) * P], qt_banks[1]).then_inc(qt_ready[1], 1)

            nc.vector.memset(warm[:], 0.0).then_inc(warm_ready, 1)
            unpack_q(0)
            unpack_q(1)
            low(0, 0)
            place_q(1)
            unpack_q(2)
            unpack_q(3)
            place_q(3)
            low(1, 0)
            unpack_q(4)
            dve.wait_ge(scale_loaded, 16)
            scale_out(0, 0, 0)
            unpack_q(5)
            unpack_q(6)
            low(2, 0)
            place_q(5)
            unpack_q(7)
            scale_out(1, 0, 0)
            dve.wait_ge(zero_loaded, 16)
            nc.vector.tensor_scalar(zs_bc[:], zs_bc[:], -1.0, QCENTER, ALU.mult, ALU.add).then_inc(zs_part, 1)
            dve.wait_ge(zs_part, 1)
            nc.vector.tensor_tensor(zs_bc[:], zs_bc[:], scale_bc[:], ALU.mult).then_inc(zs_part, 1)
            place_q(7)
            dve.wait_ge(zs_part, 2)
            for j in range(3):
                residual(j, 0)
                if j == 2:
                    scale_out(j, 0, 0)
                add_residual(j, 0, 0)
            low(3, 0)
            for j in range(3):
                finish(j, 0, 1)
                low(j + RING, 0)
            residual(3, 0)
            for h in range(H):
                finish(3, 0, h)

            def step(j, i, lows=True):
                if lows:
                    low(j + LEAD, i)
                residual(j, i)
                for h in range(H):
                    finish(j, i, h)

            with dve.Fori(1, TRIPS - 1) as i:
                for j in range(RING):
                    step(j, i)
            for j in range(RING):
                step(j, TRIPS - 1, lows=j + LEAD < RING)

        @block.gpsimd
        def _(pool):
            nc.gpsimd.memset(w_sb[:], 0.0).then_inc(w_zeroed, 1)
            nc.gpsimd.memset(ident[:], 0.0).then_inc(blank_ready, 1)
            pool.wait_ge(blank_ready, 1)
            nc.gpsimd.affine_select(out=ident[:], in_=ident[:], compare_op=ALU.not_equal, fill=1.0, base=0,
                                    pattern=[[-1, P]], channel_multiplier=1).then_inc(ident_ready, 1)
            pool.wait_ge(bias_loaded, 16)

            def add_bias(j, i):
                x_arrived(pool, j, i)
                if not isinstance(i, int) or i * RING + j >= RING:
                    for h in range(H):
                        pool.wait_ge(o_ready[h], i * RING + j - RING + 1)
                nc.gpsimd.tensor_tensor(resid[:, j % RING, :], x_sb[:, j % RING, :], bias_bc[:],
                                        ALU.add).then_inc(xbias_ready, 1)

            for j in range(RING):
                add_bias(j, 0)
            with pool.Fori(1, TRIPS) as i:
                for j in range(RING):
                    add_bias(j, i)


_INS = ['x', 'itok_B_0_15', 'L0_cond_weights', 'L0_ffn_qweight', 'L0_ffn_weight_scale',
        'L0_ffn_weight_zero_point', 'L0_ffn_bias']


def kernel(**inputs):
    import numpy as _np
    import concourse.bacc as _bacc
    from concourse import mybir as _mybir
    from concourse.bass_utils import run_bass_kernel_spmd as _run

    nc = _bacc.Bacc("TRN2", target_bir_lowering=False, num_devices=1)
    arrays, args = {}, []
    for name in _INS:
        a = _np.ascontiguousarray(inputs[name])
        arrays[f"in_{name}_dram"] = a
        args.append(nc.dram_tensor(f"in_{name}_dram", a.shape, _mybir.dt.from_np(a.dtype), kind="ExternalInput").ap())
    args.append(nc.dram_tensor("out_0_dram", inputs["x"].shape, _mybir.dt.float32, kind="ExternalOutput").ap())
    adaln_ffn(nc, *args)
    r = _run(nc, [arrays], core_ids=[0])
    return r.results[0]["out_0_dram"]
```

```python
from contextlib import ExitStack

import concourse.bass as bass
from concourse import mybir

ALU = mybir.AluOpType
ACT = mybir.ActivationFunctionType
F32 = mybir.dt.float32
F32R = mybir.dt.float32r
BF16 = mybir.dt.bfloat16
I32 = mybir.dt.int32
I16 = mybir.dt.int16

P = 128
WARMUP = 20
QCENTER = 32.0
QMASK = 63
QBITS = 6


def adaln_ffn(nc: bass.Bass, x, cond, weights, qweight, scale, zero, bias, out):
    B, C, K = x.shape
    NCOND, _, S = weights.shape
    N, KP = qweight.shape
    assert C == S == P // 2 and N == K
    G = KP // 3
    KT = K // P
    NT = N // P
    H = 2
    NH = N // H
    TILES = B // 2
    RING = 4
    LEAD = 3
    LOADLEAD = LEAD + RING
    TRIPS = TILES // RING
    assert TILES % RING == 0

    x_rows = x.rearrange("b c k -> (b c) k")
    out_rows = out.rearrange("b s n -> (b s) n")

    with ExitStack() as ctx:
        def sb(name, shape, dt):
            return ctx.enter_context(nc.sbuf_tensor(name, shape, dt))

        def psum(name, shape, dt):
            return ctx.enter_context(nc.psum_tensor(name, shape, dt))

        def sem(name):
            return ctx.enter_context(nc.semaphore(name))

        ids = sb("ids", [1, B], I32)
        x_sb = sb("x_sb", [P, RING, K], F32)
        w_sb = sb("w_sb", [P, RING, P], F32)
        y_hi = sb("y_hi", [P, RING, KT, P], F32R)
        y_lo = sb("y_lo", [P, RING, KT, P], F32R)
        qT = sb("qT", [P, KT, N], F32R)
        q_raw = sb("q_raw", [P, NT, KP], I32)
        q_int = sb("q_int", [P, 2, G, 4], I16)
        q_bf = sb("q_bf", [P, 4, K], BF16)
        ident = sb("ident", [P, P], BF16)
        scale_bc = sb("scale_bc", [P, N], F32)
        bias_bc = sb("bias_bc", [P, N], F32)
        zs_bc = sb("zs_bc", [P, N], F32)
        w_stack = sb("w_stack", [P, RING, S], F32)
        xsum = sb("xsum", [P, RING, 2], F32)
        ysum = sb("ysum", [P, RING], F32)
        warm = sb("warm", [P, 512], BF16)
        junk = sb("junk", [P, K], BF16)
        resid = sb("resid", [P, RING, N], F32)
        o_sb = sb("o_sb", [P, 2, N], F32)

        y_ps = psum("y_ps", [P, 2, KT, P], F32)
        o_ps = psum("o_ps", [P, H, NH], F32)
        ysum_ps = psum("ysum_ps", [P, 512], F32)
        qt_ps = psum("qt_ps", [P, KT, P], BF16)
        qt_banks = [qt_ps[:, :, :], o_ps[:, 1, :].bitcast(BF16).rearrange("p (t n) -> p t n", t=KT)]

        last_pieces = [(o_ps[:, 1, 0:NH // 2], NH, NH // 2),
                       (y_ps[:, 0, 0:KT // 2, :].rearrange("p t r -> p (t r)")[:, 0:NH // 2], NH + NH // 2, NH // 2)]

        ids_loaded = sem("ids_loaded")
        x_loaded = [sem(f"x_loaded{s}") for s in range(RING)]
        w_loaded = [sem(f"w_loaded{s}") for s in range(RING)]
        w_stacked = [sem(f"w_stacked{s}") for s in range(RING)]
        q_loaded = [sem(f"q_loaded{n}") for n in range(NT)]
        scale_loaded = sem("scale_loaded")
        zero_loaded = sem("zero_loaded")
        bias_loaded = sem("bias_loaded")
        w_zeroed = sem("w_zeroed")
        xsum_zeroed = sem("xsum_zeroed")
        blank_ready = sem("blank_ready")
        ident_ready = sem("ident_ready")
        zs_part = sem("zs_part")
        q_part = sem("q_part")
        q_cast = sem("q_cast")
        qt_ps_ready = sem("qt_ps_ready")
        qt_ready = sem("qt_ready")
        warm_ready = sem("warm_ready")
        y_ps_ready = sem("y_ps_ready")
        y_hi_ready = sem("y_hi_ready")
        y_lo_ready = sem("y_lo_ready")
        xsum_ready = sem("xsum_ready")
        ysum_ps_ready = sem("ysum_ps_ready")
        ysum_ready = sem("ysum_ready")
        xbias_ready = sem("xbias_ready")
        resid_ready = sem("resid_ready")
        o_ps_ready = [sem(f"o_ps_ready{h}") for h in range(H)]
        scaled = [sem(f"scaled{h}") for h in range(H)]
        o_ready = [sem(f"o_ready{h}") for h in range(H)]
        o_stored = [[sem(f"o_stored{h}_{s}") for s in range(2)] for h in range(H)]

        block = ctx.enter_context(nc.Block())

        def x_arrived(eng, j, i):
            eng.wait_ge(x_loaded[j % RING], (i + j // RING + 1) * 16)

        @block.sync
        def _(sp):
            def load_x(j, i):
                t = i * RING + j
                sp.dma_start(x_sb[:, j % RING, :],
                             x_rows[bass.ds(t * P, P), :]).then_inc(x_loaded[j % RING], 16)

            def load_w(j, i):
                t = i * RING + j
                picked = [sp.value_load(ids[0:1, bass.ds(t * 2 + half, 1)], min_val=0, max_val=NCOND - 1)
                          for half in range(2)]
                for half in range(2):
                    rows = slice(half * S, (half + 1) * S)
                    sp.dma_start(w_sb[rows, j % RING, rows],
                                 weights[bass.ds(picked[half], 1), :, :].rearrange("a c s -> (a c) s")
                                 ).then_inc(w_loaded[j % RING], 16)
                for half in range(2):
                    rows = slice(half * S, (half + 1) * S)
                    sp.dma_start(w_stack[rows, j % RING, :],
                                 weights[bass.ds(picked[half], 1), :, :].rearrange("a c s -> (a c) s")
                                 ).then_inc(w_stacked[j % RING], 16)

            def reload(j, i):
                old = i * RING + j - RING + 1
                sp.wait_ge(y_ps_ready, old * 2)
                sp.wait_ge(ysum_ps_ready, old)
                sp.wait_ge(xsum_ready, old * 2)
                sp.wait_ge(xbias_ready, old)
                load_x(j, i)
                load_w(j, i)

            def store(j, i, h):
                t = i * RING + j
                sp.wait_ge(o_ready[h], t + 1)
                sp.dma_start(out_rows[bass.ds(t * P, P), h * NH:(h + 1) * NH],
                             o_sb[:, j % 2, h * NH:(h + 1) * NH]).then_inc(o_stored[h][j % 2], 16)

            def store_last():
                t = TILES - 1
                store(t % RING, t // RING, 0)
                for n, (_, col, width) in enumerate(last_pieces):
                    sp.wait_ge(o_ready[1], t + 1 + n)
                    sp.dma_start(out_rows[t * P:(t + 1) * P, col:col + width],
                                 o_sb[:, t % 2, col:col + width]).then_inc(o_stored[1][t % 2], 16)

            def load_q(n):
                sp.dma_start(q_raw[:, n, :], qweight[n * P:(n + 1) * P, :]).then_inc(q_loaded[n], 16)

            def load_row(dst, src, s):
                sp.dma_start(dst[:], src.partition_broadcast(P)).then_inc(s, 16)

            sp.dma_start(ids[:], cond.rearrange("(a b) -> a b", a=1)).then_inc(ids_loaded, 16)
            load_x(0, 0)
            load_q(0)
            load_q(1)
            sp.wait_ge(ids_loaded, 16)
            sp.wait_ge(w_zeroed, 1)
            load_w(0, 0)
            load_x(1, 0)
            load_q(2)
            load_q(3)
            load_w(1, 0)
            load_row(scale_bc, scale.rearrange("n a -> (n a)"), scale_loaded)
            load_x(2, 0)
            load_q(4)
            load_w(2, 0)
            for n in range(5, NT):
                load_q(n)
            load_row(zs_bc, zero.rearrange("n a -> (n a)"), zero_loaded)
            load_row(bias_bc, bias, bias_loaded)
            load_x(3, 0)
            load_w(3, 0)

            for j in range(3):
                reload(j + RING, 0)
                store(j, 0, 0)
            for j in range(3):
                store(j, 0, 1)
                reload(j + LOADLEAD, 0)

            def step(j, i, loads=True):
                if loads:
                    reload(j + LOADLEAD, i)
                for h in range(H):
                    store(j, i, h)

            step(3, 0)
            with sp.Fori(1, TRIPS - 2) as i:
                for j in range(RING):
                    step(j, i)
            for t in range(TILES - 2 * RING, TILES - 1):
                step(t % RING, t // RING, loads=t + LOADLEAD < TILES)
            store_last()
            for h in range(H):
                for s in range(2):
                    stores = TILES // 2 + (len(last_pieces) - 1) * (h == 1 and s == (TILES - 1) % 2)
                    sp.wait_ge(o_stored[h][s], 16 * stores)

        @block.tensor
        def _(pe):
            def mix(j, i):
                t = i * RING + j
                slot = j % RING
                x_arrived(pe, j, i)
                pe.wait_ge(w_loaded[slot], (i + j // RING + 1) * 32)
                if not isinstance(t, int) or t >= 2:
                    pe.wait_ge(y_lo_ready, (t - 1) * 2)
                for kt in range(KT):
                    last = nc.tensor.matmul(y_ps[:, j % 2, kt, :], x_sb[:, slot, kt * P:(kt + 1) * P],
                                            w_sb[:, slot, :], start=True, stop=True)
                    if kt % (KT // 2) == KT // 2 - 1:
                        last.then_inc(y_ps_ready, 1)

            def sum_y(j, i):
                t = i * RING + j
                slot = j % RING
                pe.wait_ge(w_stacked[slot], (i + j // RING + 1) * 32)
                pe.wait_ge(xsum_ready, t * 2 + 2)
                if not isinstance(t, int) or t >= 1:
                    pe.wait_ge(ysum_ready, t * 2)
                nc.tensor.matmul(ysum_ps[0:S, 2 * slot:2 * slot + 2], w_stack[:, slot, :], xsum[:, slot, :],
                                 start=True, stop=True).then_inc(ysum_ps_ready, 1)

            def transpose_q(n):
                pe.wait_ge(q_cast, n + 1)
                if n >= 2:
                    pe.wait_ge(qt_ready, n - 1)
                for kt in range(KT):
                    last = nc.tensor.transpose(qt_banks[n % 2][:, kt, :], q_bf[:, n % 4, kt * P:(kt + 1) * P],
                                               ident[:])
                last.then_inc(qt_ps_ready, 1)

            def linear(j, i, h):
                t = i * RING + j
                if h == 0:
                    pe.wait_ge(y_lo_ready, t * 2 + 2)
                if not isinstance(t, int) or t >= 1:
                    pe.wait_ge(scaled[h], t)
                products(o_ps[:, h, :], h * NH, NH, j % RING).then_inc(o_ps_ready[h], 1)

            def products(bank, col, width, slot):
                for kt in range(KT):
                    for part in (y_hi, y_lo):
                        last = nc.tensor.matmul(bank, part[:, slot, kt, :], qT[:, kt, col:col + width],
                                                start=(kt == 0 and part is y_hi),
                                                stop=(kt == KT - 1 and part is y_lo))
                return last

            def step(j, i, mixes=True):
                if mixes:
                    mix(j + LEAD, i)
                    sum_y(j + LEAD, i)
                for h in range(H):
                    linear(j, i, h)

            pe.wait_ge(warm_ready, 1)
            for _ in range(WARMUP):
                nc.tensor.matmul(ysum_ps[:], warm[:, 0:P], warm[:], start=True, stop=True)
            mix(0, 0)
            sum_y(0, 0)
            pe.wait_ge(ident_ready, 1)
            for n in range(NT // 2):
                transpose_q(n)
            mix(1, 0)
            pe.wait_ge(qt_ready, NT // 2)
            linear(0, 0, 0)
            sum_y(1, 0)
            mix(2, 0)
            sum_y(2, 0)
            transpose_q(4)
            transpose_q(5)
            linear(1, 0, 0)
            transpose_q(6)
            transpose_q(7)
            linear(2, 0, 0)
            mix(3, 0)
            sum_y(3, 0)
            pe.wait_ge(qt_ready, NT)
            for j in range(3):
                linear(j, 0, 1)
                mix(j + RING, 0)
                sum_y(j + RING, 0)
            for h in range(H):
                linear(3, 0, h)
            with pe.Fori(1, TRIPS - 1) as i:
                for j in range(RING):
                    step(j, i)
            for j in range(RING - 1):
                step(j, TRIPS - 1, mixes=j + LEAD < RING)
            linear(RING - 1, TRIPS - 1, 0)
            pe.wait_ge(scaled[1], TILES - 1)
            for bank, col, width in last_pieces:
                products(bank, col, width, RING - 1).then_inc(o_ps_ready[1], 1)

        @block.scalar
        def _(act):
            def sum_x(j, i):
                x_arrived(act, j, i)
                if not isinstance(i, int) or i * RING + j >= RING:
                    act.wait_ge(ysum_ps_ready, i * RING + j - RING + 1)
                for half in range(2):
                    rows = slice(half * C, (half + 1) * C)
                    nc.scalar.activation(junk[rows, :], x_sb[rows, j % RING, :], ACT.Copy,
                                         accum_out=xsum[rows, j % RING, half:half + 1]).then_inc(xsum_ready, 1)

            def high(j, i):
                t = i * RING + j
                for half in range(2):
                    act.wait_ge(y_ps_ready, t * 2 + half + 1)
                    chunks = slice(half * KT // 2, (half + 1) * KT // 2)
                    nc.scalar.activation(y_hi[:, j % RING, chunks, :], y_ps[:, j % 2, chunks, :],
                                         ACT.Copy).then_inc(y_hi_ready, 1)

            def copy_ysum(j, i):
                t = i * RING + j
                act.wait_ge(ysum_ps_ready, t + 1)
                if not isinstance(t, int) or t >= RING:
                    act.wait_ge(resid_ready, t - RING + 1)
                for half in range(2):
                    col = 2 * (j % RING) + half
                    nc.scalar.activation(ysum[half * S:(half + 1) * S, j % RING:j % RING + 1],
                                         ysum_ps[0:S, col:col + 1], ACT.Copy).then_inc(ysum_ready, 1)

            def place_q(n):
                act.wait_ge(qt_ps_ready, n + 1)
                nc.scalar.activation(qT[:, :, n * P:(n + 1) * P], qt_banks[n % 2], ACT.Copy).then_inc(qt_ready, 1)

            act.wait_ge(xsum_zeroed, 1)
            sum_x(0, 0)
            high(0, 0)
            copy_ysum(0, 0)
            for n in range(NT // 2):
                place_q(n)
            high(1, 0)
            sum_x(1, 0)
            copy_ysum(1, 0)
            sum_x(2, 0)
            high(2, 0)
            copy_ysum(2, 0)
            place_q(4)
            place_q(5)
            sum_x(3, 0)
            place_q(6)
            place_q(7)
            high(3, 0)
            copy_ysum(3, 0)
            sum_x(4, 0)

            def step(j, i, highs=True, sums=True):
                if highs:
                    high(j + LEAD, i)
                    copy_ysum(j + LEAD, i)
                if sums:
                    sum_x(j + LEAD + 1, i)

            for j in range(1, RING):
                step(j, 0)
            with act.Fori(1, TRIPS - 1) as i:
                for j in range(RING):
                    step(j, i)
            step(0, TRIPS - 1, sums=False)

        @block.vector
        def _(dve):
            def unpack_q(n):
                dve.wait_ge(q_loaded[n], 16)
                words = q_raw[:, n, :].bitcast(I16).rearrange("p (g w e) -> p g w e", w=3, e=2)
                to = q_int[:, n % 2, :, :]
                if n >= 2:
                    dve.wait_ge(q_cast, n - 1)
                nc.vector.tensor_scalar(to[:, :, 0], words[:, :, 0, 0], QMASK, None,
                                        ALU.bitwise_and).then_inc(q_part, 1)
                nc.vector.tensor_scalar(to[:, :, 1], words[:, :, 0, 0], QBITS, QMASK,
                                        ALU.logical_shift_right, ALU.bitwise_and).then_inc(q_part, 1)
                nc.vector.tensor_scalar(to[:, :, 2:4], words[:, :, 1:3, 0], QMASK, None,
                                        ALU.bitwise_and).then_inc(q_part, 1)
                dve.wait_ge(q_part, 3 * (n + 1))
                if n >= 4:
                    dve.wait_ge(qt_ps_ready, n - 3)
                nc.vector.tensor_scalar(q_bf[:, n % 4, :], to.rearrange("p g j -> p (g j)"), QCENTER, None,
                                        ALU.subtract).then_inc(q_cast, 1)

            def low(j, i):
                t = i * RING + j
                for half in range(2):
                    dve.wait_ge(y_hi_ready, t * 2 + half + 1)
                    chunks = slice(half * KT // 2, (half + 1) * KT // 2)
                    nc.vector.tensor_tensor(y_lo[:, j % RING, chunks, :], y_ps[:, j % 2, chunks, :],
                                            y_hi[:, j % RING, chunks, :].bitcast(F32),
                                            ALU.subtract).then_inc(y_lo_ready, 1)

            def residual(j, i):
                t = i * RING + j
                dve.wait_ge(xbias_ready, t + 1)
                dve.wait_ge(ysum_ready, t * 2 + 2)
                nc.vector.scalar_tensor_tensor(resid[:, j % RING, :], zs_bc[:], ysum[:, j % RING:j % RING + 1],
                                               resid[:, j % RING, :], ALU.mult, ALU.add).then_inc(resid_ready, 1)

            def scale_out(j, i, h):
                t = i * RING + j
                cols = slice(h * NH, (h + 1) * NH)
                dve.wait_ge(o_ps_ready[h], t + 1)
                if not isinstance(i, int):
                    dve.wait_ge(o_stored[h][j % 2], (i * (RING // 2) + j // 2) * 16)
                elif t >= 2:
                    dve.wait_ge(o_stored[h][j % 2], t // 2 * 16)
                nc.vector.tensor_tensor(o_sb[:, j % 2, cols], o_ps[:, h, :], scale_bc[:, cols],
                                        ALU.mult).then_inc(scaled[h], 1)

            def add_residual(j, i, h):
                t = i * RING + j
                cols = slice(h * NH, (h + 1) * NH)
                dve.wait_ge(scaled[h], t + 1)
                dve.wait_ge(resid_ready, t + 1)
                nc.vector.tensor_tensor(o_sb[:, j % 2, cols], o_sb[:, j % 2, cols],
                                        resid[:, j % RING, cols], ALU.add).then_inc(o_ready[h], 1)

            def finish(j, i, h):
                scale_out(j, i, h)
                add_residual(j, i, h)

            nc.vector.memset(xsum[:], 0.0).then_inc(xsum_zeroed, 1)
            nc.vector.memset(warm[:], 0.0).then_inc(warm_ready, 1)
            for n in range(NT // 2):
                unpack_q(n)
            low(0, 0)
            low(1, 0)
            unpack_q(4)
            dve.wait_ge(scale_loaded, 16)
            scale_out(0, 0, 0)
            unpack_q(5)
            unpack_q(6)
            low(2, 0)
            unpack_q(7)
            scale_out(1, 0, 0)
            dve.wait_ge(zero_loaded, 16)
            nc.vector.tensor_scalar(zs_bc[:], zs_bc[:], -1.0, QCENTER, ALU.mult, ALU.add).then_inc(zs_part, 1)
            dve.wait_ge(zs_part, 1)
            nc.vector.tensor_tensor(zs_bc[:], zs_bc[:], scale_bc[:], ALU.mult).then_inc(zs_part, 1)
            dve.wait_ge(zs_part, 2)
            for j in range(3):
                residual(j, 0)
                if j == 2:
                    scale_out(j, 0, 0)
                add_residual(j, 0, 0)
            low(3, 0)
            for j in range(3):
                finish(j, 0, 1)
                low(j + RING, 0)
            residual(3, 0)
            for h in range(H):
                finish(3, 0, h)

            def step(j, i, lows=True):
                if lows:
                    low(j + LEAD, i)
                residual(j, i)
                for h in range(H):
                    finish(j, i, h)

            with dve.Fori(1, TRIPS - 1) as i:
                for j in range(RING):
                    step(j, i)
            for j in range(RING - 1):
                step(j, TRIPS - 1, lows=j + LEAD < RING)
            residual(RING - 1, TRIPS - 1)
            finish(RING - 1, TRIPS - 1, 0)
            t = TILES - 1
            dve.wait_ge(o_stored[1][t % 2], t // 2 * 16)
            for n, (bank, col, width) in enumerate(last_pieces):
                cols = slice(col, col + width)
                dve.wait_ge(o_ps_ready[1], t + 1 + n)
                nc.vector.tensor_tensor(o_sb[:, t % 2, cols], bank, scale_bc[:, cols], ALU.mult).then_inc(scaled[1], 1)
                dve.wait_ge(scaled[1], t + 1 + n)
                nc.vector.tensor_tensor(o_sb[:, t % 2, cols], o_sb[:, t % 2, cols], resid[:, t % RING, cols],
                                        ALU.add).then_inc(o_ready[1], 1)

        @block.gpsimd
        def _(pool):
            nc.gpsimd.memset(w_sb[:], 0.0).then_inc(w_zeroed, 1)
            nc.gpsimd.memset(ident[:], 0.0).then_inc(blank_ready, 1)
            pool.wait_ge(blank_ready, 1)
            nc.gpsimd.affine_select(out=ident[:], in_=ident[:], compare_op=ALU.not_equal, fill=1.0, base=0,
                                    pattern=[[-1, P]], channel_multiplier=1).then_inc(ident_ready, 1)
            pool.wait_ge(bias_loaded, 16)

            def add_bias(j, i):
                x_arrived(pool, j, i)
                if not isinstance(i, int) or i * RING + j >= RING:
                    for h in range(H):
                        pool.wait_ge(o_ready[h], i * RING + j - RING + 1)
                nc.gpsimd.tensor_tensor(resid[:, j % RING, :], x_sb[:, j % RING, :], bias_bc[:],
                                        ALU.add).then_inc(xbias_ready, 1)

            for j in range(RING):
                add_bias(j, 0)
            with pool.Fori(1, TRIPS) as i:
                for j in range(RING):
                    add_bias(j, i)


_INS = ['x', 'itok_B_0_15', 'L0_cond_weights', 'L0_ffn_qweight', 'L0_ffn_weight_scale',
        'L0_ffn_weight_zero_point', 'L0_ffn_bias']


def kernel(**inputs):
    import numpy as _np
    import concourse.bacc as _bacc
    from concourse import mybir as _mybir
    from concourse.bass_utils import run_bass_kernel_spmd as _run

    nc = _bacc.Bacc("TRN2", target_bir_lowering=False, num_devices=1)
    arrays, args = {}, []
    for name in _INS:
        a = _np.ascontiguousarray(inputs[name])
        arrays[f"in_{name}_dram"] = a
        args.append(nc.dram_tensor(f"in_{name}_dram", a.shape, _mybir.dt.from_np(a.dtype), kind="ExternalInput").ap())
    args.append(nc.dram_tensor("out_0_dram", inputs["x"].shape, _mybir.dt.float32, kind="ExternalOutput").ap())
    adaln_ffn(nc, *args)
    r = _run(nc, [arrays], core_ids=[0])
    return r.results[0]["out_0_dram"]
```
